# Optimizing a Trainium2 kernel written in Bass

```python
import numpy as np
import jax
import jax.numpy as jnp

def _softmax(x, axis=-1):
    return jax.nn.softmax(x, axis=axis)

def _gelu(x):
    return jax.nn.gelu(x, approximate=True)

def _silu(x):
    return jax.nn.silu(x)

def _sigmoid(x):
    return jax.nn.sigmoid(x)

def _layernorm(x, axis=-1, eps=1e-05):
    m = jnp.mean(x, axis=axis, keepdims=True)
    v = jnp.var(x, axis=axis, keepdims=True)
    return (x - m) / jnp.sqrt(v + eps)

def _scatter_add(tgt, idx, src, axis=0):
    return tgt.at[idx].add(src)

def _segment_sum(src, seg, n):
    return jax.ops.segment_sum(src, seg, n)
kernel_name = 'mk_cond_resid_d2_seqx_r4_0dcb30'

def setup_inputs(seed: int=0):
    np.random.seed(seed)
    _w = jnp.asarray

    def _rec_inputs():
        import jax
        import jax.numpy as jnp
        _rk = jax.random.key(seed)
        x = -0.000125 + 0.9999 * jax.random.normal(jax.random.fold_in(_rk, 1), (2, 1024, 256), jnp.float32)
        _lenS = 1024 - jax.random.randint(jax.random.fold_in(_rk, 7), (2,), 0, max(1, 1024 // 4) + 1, jnp.int32)
        _lenS2 = 1024 - jax.random.randint(jax.random.fold_in(_rk, 8), (2,), 0, max(1, 1024 // 4) + 1, jnp.int32)
        cond_1024 = -0.00493535 + 1.00056 * jax.random.normal(jax.random.fold_in(_rk, 11), (2, 256), jnp.float32)
        return (x, cond_1024)
    x, cond_1024 = _rec_inputs()

    def _L0_cond_setup():
        import jax, jax.numpy as jnp
        import numpy as np
        N, T, D, H = (64, 128, 256, 256)

        def lstm_scan(x, h0, Wx, Wh, b):
            xW = jnp.einsum('ntd,dg->ntg', x, Wx) + b
            Hdim = h0.shape[1]
            c0 = jnp.zeros_like(h0)

            def step(carry, xw_t):
                prev_h, prev_c = carry
                a = xw_t + prev_h @ Wh
                i = jax.nn.sigmoid(a[:, :Hdim])
                f = jax.nn.sigmoid(a[:, Hdim:2 * Hdim])
                o = jax.nn.sigmoid(a[:, 2 * Hdim:3 * Hdim])
                g = jnp.tanh(a[:, 3 * Hdim:])
                next_c = f * prev_c + i * g
                next_h = o * jnp.tanh(next_c)
                return ((next_h, next_c), next_h)
            _, hs = jax.lax.scan(step, (h0, c0), jnp.swapaxes(xW, 0, 1))
            return jnp.swapaxes(hs, 0, 1)
        key = jax.random.key(seed)
        k1, k2, k3, k4 = jax.random.split(key, 4)
        x = jax.random.normal(k1, (N, T, D), dtype=jnp.float32)
        h0 = jax.random.normal(k2, (N, H), dtype=jnp.float32)
        Wx = jax.random.normal(k3, (D, 4 * H), dtype=jnp.float32) / np.sqrt(D)
        Wh = jax.random.normal(k4, (H, 4 * H), dtype=jnp.float32) / np.sqrt(H)
        b = jnp.zeros((4 * H,), dtype=jnp.float32)
        return {'x': x, 'h0': h0, 'Wx': Wx, 'Wh': Wh, 'b': b}
    _L0_cond_all = _L0_cond_setup()
    _L0_cond_in = {k: v for k, v in _L0_cond_all.items() if k in ('Wx', 'Wh', 'b')}
    del _L0_cond_all

    def _L1_cond_setup():
        import jax, jax.numpy as jnp
        import numpy as np
        IN_FEATURES = 256
        OUT_FEATURES = 256
        BATCH = 32
        SEQ = 256
        EPS = 1e-08
        key = jax.random.key(seed)
        k1, k2, k3 = jax.random.split(key, 3)
        Efou = jax.random.normal(k1, (BATCH, SEQ, IN_FEATURES), dtype=jnp.float32)
        y = jax.random.normal(k2, (BATCH, IN_FEATURES), dtype=jnp.float32)
        weight = jax.random.normal(k3, (IN_FEATURES, OUT_FEATURES), dtype=jnp.float32)
        return {'Efou': Efou, 'y': y, 'weight': weight}
    _L1_cond_all = _L1_cond_setup()
    _L1_cond_in = {k: v for k, v in _L1_cond_all.items() if k in ('weight',)}
    del _L1_cond_all
    return {'x': x, 'cond_1024': cond_1024, 'L0_cond_Wx': _L0_cond_in['Wx'], 'L0_cond_Wh': _L0_cond_in['Wh'], 'L0_cond_b': _L0_cond_in['b'], 'L1_cond_weight': _L1_cond_in['weight']}

def reference(x, cond_1024, L0_cond_Wx, L0_cond_Wh, L0_cond_b, L1_cond_weight):
    import jax
    import jax.numpy as jnp

    def _L0_cond_ref(x, h0, Wx, Wh, b):
        import jax, jax.numpy as jnp
        import numpy as np
        N, T, D, H = (64, 128, 256, 256)

        def lstm_scan(x, h0, Wx, Wh, b):
            xW = jnp.einsum('ntd,dg->ntg', x, Wx) + b
            Hdim = h0.shape[1]
            c0 = jnp.zeros_like(h0)

            def step(carry, xw_t):
                prev_h, prev_c = carry
                a = xw_t + prev_h @ Wh
                i = jax.nn.sigmoid(a[:, :Hdim])
                f = jax.nn.sigmoid(a[:, Hdim:2 * Hdim])
                o = jax.nn.sigmoid(a[:, 2 * Hdim:3 * Hdim])
                g = jnp.tanh(a[:, 3 * Hdim:])
                next_c = f * prev_c + i * g
                next_h = o * jnp.tanh(next_c)
                return ((next_h, next_c), next_h)
            _, hs = jax.lax.scan(step, (h0, c0), jnp.swapaxes(xW, 0, 1))
            return jnp.swapaxes(hs, 0, 1)
        return lstm_scan(x, h0, Wx, Wh, b)

    def _L1_cond_ref(Efou, y, weight):
        import jax, jax.numpy as jnp
        import numpy as np
        IN_FEATURES = 256
        OUT_FEATURES = 256
        BATCH = 32
        SEQ = 256
        EPS = 1e-08
        scale = 1.0 / np.sqrt(np.float32(weight.shape[0]))
        ys = y * scale
        d = jax.lax.rsqrt(jnp.einsum('bi,io->bo', ys * ys, weight * weight) + EPS)
        out = jnp.einsum('bsi,io->bso', Efou * ys[:, None, :], weight) * d[:, None, :]
        return out
    x = x + _L0_cond_ref(x, cond_1024, L0_cond_Wx, L0_cond_Wh, L0_cond_b)
    x = x + _L1_cond_ref(x, cond_1024, L1_cond_weight)
    return x

_drawn_inputs = setup_inputs


def setup_inputs(seed=0):
    import zlib

    import numpy as np

    out = dict(_drawn_inputs(seed))
    spreads = {'L0_cond_b': (0.0, 0.1)}
    factors = {}
    for name, (base, spread) in spreads.items():
        noise = np.random.default_rng([zlib.crc32(name.encode()), seed]).standard_normal(out[name].shape)
        drawn = base * np.exp(spread * noise) if base else spread * noise
        out[name] = jnp.asarray(drawn.astype(out[name].dtype))
    for name, factor in factors.items():
        out[name] = (out[name] * factor).astype(out[name].dtype)
    return out
```

```python
import concourse.bass as bass
from concourse import mybir
from contextlib import ExitStack

P = 128
F32 = mybir.dt.float32
ACT = mybir.ActivationFunctionType
ALU = mybir.AluOpType


def build(nc, x, cond, Wx, Wh, b, w, out):
    B, SEQ, D = x.shape
    K = D // P
    G = 4
    I_, F_, O_, G_ = range(G)
    T = 32
    SETS = 2
    BODY = SETS * T
    NBLK = SEQ // T
    COLS = T * B
    AG = (F_, I_, G_)
    NA = len(AG)
    XL = 2
    TT = SEQ // P

    ctx = ExitStack()
    with ctx:
        def sb(name, shape):
            return ctx.enter_context(nc.sbuf_tensor(name, shape, F32))

        def sem(name):
            return ctx.enter_context(nc.semaphore(name))

        wx_sb = sb("wx_sb", [P, K, G * D])
        wh_sb = sb("wh_sb", [P, K, G * D])
        bias_sb = sb("bias_sb", [P, G * D])
        ones = sb("ones", [P, P])
        ident = sb("ident", [P, P])
        xrow = sb("xrow", [P, B, TT, D])
        xT = sb("xT", [P, K, SEQ + T, B])
        xblk = sb("xblk", [P, SETS, K, T, B])
        hblk = sb("hblk", [P, SETS, T, K, B])
        hist = sb("hist", [P, SEQ, K, B])
        gates = sb("gates", [P, K, NA, B, 2])
        ogate = sb("ogate", [P, K, B])
        cell = sb("cell", [P, K, 2, 8])
        tanhc = sb("tanhc", [P, K, B])
        condT = sb("condT", [P, K, B])
        ysq = sb("ysq", [P, K, B])
        yscale = sb("yscale", [P, K, B])
        w_sb = sb("w_sb", [P, K, D])
        wsq = sb("wsq", [P, K, D])
        dm = sb("dm", [P, B, D])
        wmod = sb("wmod", [P, B, K, D])
        ores = sb("ores", [P, B, TT, D])

        pA = [[ctx.enter_context(nc.psum_tensor(f"pA{s}{j}", [P, T, NA, B], F32)) for j in range(K)] for s in range(SETS)]
        pO = [ctx.enter_context(nc.psum_tensor(f"pO{s}", [P, T, K, B], F32)) for s in range(SETS)]
        pX = [ctx.enter_context(nc.psum_tensor(f"pX{s}", [P, 512], F32)) for s in range(2)]

        s_wx, s_wh, s_b, s_c, s_w, s_out = (sem(n) for n in ("s_wx", "s_wh", "s_b", "s_c", "s_w", "s_out"))
        s_x = [sem(f"s_x{n}") for n in range(B * XL)]
        s_ms, s_id, s_xT, s_xTc, s_scale, s_setup = (sem(n) for n in ("s_ms", "s_id", "s_xT", "s_xTc", "s_scale", "s_setup"))
        s_xb, s_fill, s_hcopied = (sem(n) for n in ("s_xb", "s_fill", "s_hcopied"))
        s_a = [sem(f"s_a{j}") for j in range(K)]
        s_o = sem("s_o")
        s_sa = [sem(f"s_sa{j}") for j in range(K)]
        s_so = sem("s_so")
        s_u = [sem(f"s_u{j}") for j in range(K)]
        s_cell = [sem(f"s_cell{j}") for j in range(K)]
        s_th = [sem(f"s_th{j}") for j in range(K)]
        s_h = [sem(f"s_h{j}") for j in range(K)]
        s_ysq, s_dmp, s_sqrt, s_dm, s_wm, s_xn, s_y, s_yc = (sem(n) for n in ("s_ysq", "s_dmp", "s_sqrt", "s_dm", "s_wm", "s_xn", "s_y", "s_yc"))
        s_yd = sem("s_yd")
        s_yr = sem("s_yr")

        block = ctx.enter_context(nc.Block())
        NX = B * TT
        NXT = NX * K

        def prev(blk, ls):
            st, t = divmod(ls - 1, T)
            return hblk[:, st % SETS, t, :, :]

        @block.sync
        def _(sp):
            for n in range(B * XL):
                bb, lo = n // XL, n % XL * (TT // XL)
                sp.dma_start(xrow[:, bb, lo:lo + TT // XL, :],
                             x[bb, lo * P:(lo + TT // XL) * P, :].rearrange("(n p) d -> p n d", p=P)).then_inc(s_x[n], 16)
                if n == 0:
                    sp.dma_start(wx_sb[:, :, :], Wx.rearrange("(k p) g -> p k g", p=P)).then_inc(s_wx, 16)
                    sp.dma_start(wh_sb[:, :, :], Wh.rearrange("(k p) g -> p k g", p=P)).then_inc(s_wh, 16)
            for n in range(NX):
                bb, tt = n // TT, n % TT
                sp.wait_ge(s_yc, n + 1)
                sp.dma_start(out[bb, tt * P:(tt + 1) * P, :], ores[:, bb, tt, :]).then_inc(s_out, 16)
            sp.wait_ge(s_out, 16 * NX)

        @block.gpsimd
        def _(pool):
            pool.memset(ident[:, :], 0.0).then_inc(s_ms, 1)
            pool.wait_ge(s_ms, 1)
            pool.affine_select(out=ident[:, :], in_=ident[:, :], compare_op=ALU.not_equal, fill=1.0,
                               base=0, pattern=[[-1, P]], channel_multiplier=1).then_inc(s_id, 1)
            pool.memset(xT[:, :, SEQ:SEQ + T, :], 0.0).then_inc(s_xb, 1)
            pool.wait_ge(s_xTc, NXT)
            pool.tensor_copy(xblk[:, 0, :, :, :], xT[:, :, 0:T, :]).then_inc(s_xb, 1)
            with pool.Fori(0, NBLK // SETS) as it:
                i = it * SETS
                for st in range(SETS):
                    if st == 0:
                        pool.wait_ge(s_fill, i)
                    else:
                        pool.wait_ge(s_fill, i + 1)
                    pool.tensor_copy(xblk[:, 1 - st, :, :, :], xT[:, :, bass.ds((i + (st + 1)) * T, T), :]).then_inc(s_xb, 1)
                    for j in range(K):
                        pool.wait_ge(s_h[j], (i + (st + 1)) * T + 1)
                    pool.tensor_copy(hist[:, bass.ds((i + st) * T, T), :, :], hblk[:, st, :, :, :]).then_inc(s_hcopied, 1)

        @block.scalar
        def _(act):
            for bb in range(B):
                act.dma_start(condT[:, :, bb], cond[bb, :].rearrange("(k p) -> p k", p=P),
                              allow_slow_non_contiguous=True).then_inc(s_c, 16)
            act.wait_ge(s_setup, 1)
            act.dma_start(bias_sb[0:1, :], b.rearrange("(a n) -> a n", a=1)).then_inc(s_b, 16)
            act.dma_start(w_sb[:, :, :], w.rearrange("(k p) o -> p k o", p=P)).then_inc(s_w, 16)
            act.wait_ge(s_dmp, 1)
            act.activation(dm[:, :, :], pX[0][:, :].rearrange("p (b d) -> p b d", b=B), ACT.Sqrt).then_inc(s_sqrt, 1)
            with act.Fori(0, SEQ, BODY) as i:
                for ls in range(BODY):
                    st, t = divmod(ls, T)
                    for j in range(K):
                        act.wait_ge(s_a[j], i + (ls + 1))
                        act.activation(gates[:, j, :, :, 1], pA[st][j][:, t, :, :], ACT.Sigmoid).then_inc(s_sa[j], 1)
                    act.wait_ge(s_cell[0], i + (ls + 1))
                    act.activation(tanhc[:, 0, :], cell[:, 0, 1 - ls % 2, 2:6:2], ACT.Tanh, scale=2.0).then_inc(s_th[0], 1)
                    act.wait_ge(s_o, i + (ls + 1))
                    act.activation(ogate[:, :, :], pO[st][:, t, :, :], ACT.Sigmoid).then_inc(s_so, 1)
                    act.wait_ge(s_cell[1], i + (ls + 1))
                    act.activation(tanhc[:, 1, :], cell[:, 1, 1 - ls % 2, 2:6:2], ACT.Tanh, scale=2.0).then_inc(s_th[1], 1)
            for n in range(NX):
                act.wait_ge(s_y, n + 1)
                act.activation(ores[:, n // TT, n % TT, :], pX[n % 2][:, 0:D], ACT.Copy).then_inc(s_yc, 1)

        @block.tensor
        def _(pe):
            pe.wait_ge(s_id, 1)
            for n in range(NX):
                if n % (TT // XL) == 0:
                    pe.wait_ge(s_x[n // (TT // XL)], 16)
                bb, tt = n // TT, n % TT
                for k in range(K):
                    m = n * K + k
                    if m >= 2:
                        pe.wait_ge(s_xTc, m - 1)
                    pe.transpose(pX[m % 2][:, 0:P], xrow[:, bb, tt, k * P:(k + 1) * P], ident[:, :]).then_inc(s_xT, 1)
            pe.wait_ge(s_ysq, 1)
            pe.wait_ge(s_xTc, NXT)
            for bb in range(B):
                for k in range(K):
                    last = pe.matmul(pX[0][:, bb * D:(bb + 1) * D], ysq[:, k, bb:bb + 1].broadcast_to([P, P]), wsq[:, k, :],
                                     start=(k == 0), stop=(k == K - 1))
            last.then_inc(s_dmp, 1)

            def chunk(q, j):
                return slice(q * D + j * P, q * D + (j + 1) * P)

            def dest(st, q, j, lo, hi):
                if q == O_:
                    return pO[st][:, lo:hi, j, :]
                return pA[st][j][:, lo:hi, AG.index(q), :]

            def fillers(st):
                first = {}
                todo = []
                for j in range(K):
                    for q in (F_, I_, G_, O_):
                        bank = "o" if q == O_ else j
                        todo.append((q, j, None, bank not in first))
                        first[bank] = True
                        for k in range(K):
                            todo.append((q, j, k, False))
                out = []
                for q, j, k, start in todo:
                    def one(q=q, j=j, k=k, start=start):
                        d = dest(st, q, j, 0, T)
                        if k is None:
                            return pe.matmul(d, bias_sb[:, chunk(q, j)], ones[:, 0:COLS], start=start, stop=False,
                                             skip_group_check=True)
                        return pe.matmul(d, wx_sb[:, k, chunk(q, j)], xblk[:, st, k, :, :], start=False, stop=False,
                                         skip_group_check=True)
                    out.append(one)
                return out

            def rec(st, t, q, j, k, h):
                return pe.matmul(dest(st, q, j, t, t + 1), wh_sb[:, k, chunk(q, j)], h[:, k, :], start=False, stop=True,
                                 skip_group_check=True)

            pe.wait_ge(s_scale, 3)
            pe.wait_ge(s_xb, 2)
            for f in fillers(0):
                last = f()
            last.then_inc(s_fill, 1)
            with pe.Fori(0, SEQ, BODY) as i:
                for ls in range(BODY):
                    st, t = divmod(ls, T)
                    h = prev(0, ls)
                    if t == 0:
                        todo = fillers(1 - st)
                    pe.wait_ge(s_h[0], i + (ls + 1))
                    for j in range(K):
                        for q in AG:
                            rec(st, t, q, j, 0, h)
                    pe.wait_ge(s_h[1], i + (ls + 1))
                    for j in range(K):
                        for q in AG:
                            last = rec(st, t, q, j, 1, h)
                        last.then_inc(s_a[j], 1)
                    for k in range(K):
                        for j in range(K):
                            last = rec(st, t, O_, j, k, h)
                    last.then_inc(s_o, 1)
                    if t >= T - len(todo) - 1 and t < T - 1:
                        n = t - (T - len(todo) - 1)
                        if n == 0:
                            pe.wait_ge(s_xb, i // T + (st + 3))
                        last = todo[n]()
                        if n == len(todo) - 1:
                            last.then_inc(s_fill, 1)
            pe.wait_ge(s_wm, B * K)
            for n in range(NX):
                bb, tt = n // TT, n % TT
                pe.wait_ge(s_xn, 1)
                if n >= 2:
                    pe.wait_ge(s_yc, n - 1)
                for k in range(K):
                    xs = xT[:, k, tt * P:(tt + 1) * P, bb]
                    pe.matmul(pX[n % 2][:, 0:D], xs, wmod[:, bb, k, :], start=(k == 0), stop=False, skip_group_check=True)
                for k in range(K):
                    xs = xT[:, k, tt * P:(tt + 1) * P, bb]
                    last = pe.matmul(pX[n % 2][:, k * P:(k + 1) * P], xs, ident[:, :], start=False, stop=(k == K - 1), skip_group_check=True)
                last.then_inc(s_y, 1)

        @block.vector
        def _(dve):
            dve.memset(bias_sb[:, :], 0.0).then_inc(s_setup, 1)
            dve.memset(ones[:, :], 1.0).then_inc(s_scale, 1)
            dve.memset(gates[:, :, :, :, :], 0.0)
            dve.memset(cell[:, :, :, :], 0.0).then_inc(s_setup, 1)
            for n in range(NX):
                bb, tt = n // TT, n % TT
                for k in range(K):
                    m = n * K + k
                    dve.wait_ge(s_xT, m + 1)
                    dve.tensor_copy(xT[:, k, tt * P:(tt + 1) * P, bb], pX[m % 2][:, 0:P]).then_inc(s_xTc, 1)
            dve.wait_ge(s_c, 16 * B)
            dve.tensor_copy(hblk[:, SETS - 1, T - 1, :, :], condT[:, :, :])
            dve.tensor_scalar(yscale[:, :, :], condT[:, :, :], 1.0 / D ** 0.5, None, ALU.mult).then_inc(s_yd, 1)
            dve.wait_ge(s_yd, 1)
            dve.tensor_tensor(ysq[:, :, :], yscale[:, :, :], yscale[:, :, :], ALU.mult).then_inc(s_yd, 1)
            dve.wait_ge(s_yd, 2)
            dve.wait_ge(s_w, 16)
            dve.tensor_tensor(wsq[:, :, :], w_sb[:, :, :], w_sb[:, :, :], ALU.mult).then_inc(s_ysq, 1)
            dve.wait_ge(s_wx, 16)
            dve.wait_ge(s_wh, 16)
            dve.wait_ge(s_b, 16)
            gsl = slice(G_ * D, (G_ + 1) * D)
            dve.tensor_scalar(bias_sb[:, gsl], bias_sb[:, gsl], 2.0, None, ALU.mult)
            dve.tensor_scalar(wx_sb[:, :, gsl], wx_sb[:, :, gsl], 2.0, None, ALU.mult).then_inc(s_scale, 1)
            dve.tensor_scalar(wh_sb[:, :, gsl], wh_sb[:, :, gsl], 2.0, None, ALU.mult).then_inc(s_scale, 1)
            dve.wait_ge(s_sqrt, 1)
            dve.reciprocal(dm[:, :, :], dm[:, :, :]).then_inc(s_dm, 1)
            dve.wait_ge(s_dm, 1)
            for bb in range(B):
                for k in range(K):
                    dve.scalar_tensor_tensor(out=wmod[:, bb, k, :], in0=w_sb[:, k, :], scalar=yscale[:, k, bb:bb + 1],
                                             in1=dm[:, bb, :], op0=ALU.mult, op1=ALU.mult).then_inc(s_wm, 1)
            for j in range(K):
                dve.wait_ge(s_wm, B * K)
                dve.memset(tanhc[:, j, :], 0.0).then_inc(s_h[j], 1)
            with dve.Fori(0, SEQ, BODY) as i:
                for ls in range(BODY):
                    st, t = divmod(ls, T)
                    par = ls % 2
                    if t == 0:
                        if st == 1:
                            dve.wait_ge(s_hcopied, i // T)
                        else:
                            dve.wait_ge(s_hcopied, i // T)
                    for j in range(K):
                        dve.wait_ge(s_sa[j], i + (ls + 1))
                        dve.scalar_tensor_tensor(out=cell[:, j, par, 3:7:2], in0=gates[:, j, 2, :, 1], scalar=-0.5,
                                                 in1=gates[:, j, 1, :, 1], op0=ALU.add, op1=ALU.mult).then_inc(s_u[j], 1)
                        dve.wait_ge(s_u[j], i + (ls + 1))
                        dve.tensor_tensor_scan(cell[:, j, 1 - par, 1:5], gates[:, j, 0, :, :].rearrange("p b c -> p (b c)"),
                                               cell[:, j, par, 2:6], 0.0, ALU.mult, ALU.add).then_inc(s_cell[j], 1)
                    for j in range(K):
                        dve.wait_ge(s_th[j], i + (ls + 1))
                        if j == 0:
                            dve.wait_ge(s_so, i + (ls + 1))
                        dve.tensor_tensor(hblk[:, st, t, j, :], tanhc[:, j, :], ogate[:, j, :], ALU.mult).then_inc(s_h[j], 1)
            dve.wait_ge(s_hcopied, NBLK)
            dve.tensor_tensor(xT[:, :, 0:SEQ, :], xT[:, :, 0:SEQ, :], hist[:, :, :, :].rearrange("p t k b -> p k t b"),
                              ALU.add).then_inc(s_xn, 1)


_INS = ['x', 'cond_1024', 'L0_cond_Wx', 'L0_cond_Wh', 'L0_cond_b', 'L1_cond_weight']
_OUTS = [((2, 1024, 256), 'float32')]


def kernel(**inputs):
    import numpy as _np
    import concourse.bacc as _bacc
    from concourse import mybir as _mybir
    from concourse.bass_utils import run_bass_kernel_spmd as _run

    nc = _bacc.Bacc("TRN2", target_bir_lowering=False, num_devices=1)
    arrays, args = {}, []
    for name in _INS:
        a = _np.ascontiguousarray(inputs[name])
        arrays[f"in_{name}_dram"] = a
        args.append(nc.dram_tensor(f"in_{name}_dram", a.shape, _mybir.dt.from_np(a.dtype), kind="ExternalInput").ap())
    for i, (shape, dtype) in enumerate(_OUTS):
        dt = _mybir.dt.from_np(_np.dtype(dtype))
        args.append(nc.dram_tensor(f"out_{i}_dram", shape, dt, kind="ExternalOutput").ap())
    build(nc, *args)
    r = _run(nc, [arrays], core_ids=[0])
    got = tuple(r.results[0][f"out_{i}_dram"] for i in range(len(_OUTS)))
    return got[0]
```

```python
import concourse.bass as bass
from concourse import mybir
from contextlib import ExitStack

P = 128
F32 = mybir.dt.float32
ACT = mybir.ActivationFunctionType
ALU = mybir.AluOpType


def build(nc, x, cond, Wx, Wh, b, w, out):
    B, SEQ, D = x.shape
    K = D // P
    G = 4
    Q = P // G
    T = Q // B
    SETS = 2
    BODY = SETS * T
    NBLK = SEQ // T
    XL = 2
    TT = SEQ // P
    NX = B * TT
    NXT = NX * K
    I_, F_, O_, G_ = range(G)
    NU, NF = 3 * B, 2 * B
    NT = NU + NF + B
    SEL = ([(3 * bb + 1, G_, bb) for bb in range(B)] + [(3 * bb + 2, I_, bb) for bb in range(B)]
           + [(NU + 2 * bb + 1, F_, bb) for bb in range(B)] + [(NU + NF + bb, O_, bb) for bb in range(B)])
    CW, C0 = 16, 3

    WARM = 2
    XS = 64
    TM = 64
    HC = 2 * K

    ctx = ExitStack()
    with ctx:
        def sb(name, shape):
            return ctx.enter_context(nc.sbuf_tensor(name, shape, F32))

        def sem(name):
            return ctx.enter_context(nc.semaphore(name))

        wx_sb = sb("wx_sb", [P, K, G * D])
        wh_sb = sb("wh_sb", [P, K, G * D])
        bias_sb = sb("bias_sb", [P, G * D])
        ready = sb("ready", [P, HC])
        ones = sb("ones", [P, Q])
        ident = sb("ident", [P, P])
        sel = sb("sel", [P, T, NT])
        xrow = sb("xrow", [P, B, TT, D])
        xT = sb("xT", [P, K, SEQ + T, B])
        xblk = sb("xblk", [P, SETS, K, T, B])
        hst = sb("hst", [P, SETS, K, T * (Q + B)])
        hist = sb("hist", [P, SEQ, K, B])
        gates = sb("gates", [P, K, P])
        ucst = sb("ucst", [P, NU])
        cell = sb("cell", [P, K, CW])
        tanhc = sb("tanhc", [P, K, B])
        condT = sb("condT", [P, K, B])
        ysq = sb("ysq", [P, K, B])
        yscale = sb("yscale", [P, K, B])
        w_sb = sb("w_sb", [P, K, D])
        wsq = sb("wsq", [P, K, D])
        dm = sb("dm", [P, B, D])
        wmod = sb("wmod", [P, B, K, D])
        ores = sb("ores", [P, B, TT, D])

        pA = [[ctx.enter_context(nc.psum_tensor(f"pA{s}{j}", [P, 512], F32)) for j in range(K)] for s in range(SETS)]
        pT = [ctx.enter_context(nc.psum_tensor(f"pT{j}", [P, 512], F32)) for j in range(K)]
        pX = [ctx.enter_context(nc.psum_tensor(f"pX{s}", [P, 512], F32)) for s in range(2)]

        s_wx, s_wh, s_b, s_c, s_w, s_out = (sem(n) for n in ("s_wx", "s_wh", "s_b", "s_c", "s_w", "s_out"))
        s_x = [sem(f"s_x{n}") for n in range(B * XL)]
        s_ms, s_id, s_xT, s_xTc, s_scale, s_setup = (sem(n) for n in ("s_ms", "s_id", "s_xT", "s_xTc", "s_scale", "s_setup"))
        s_xb, s_fill, s_hcopied = (sem(n) for n in ("s_xb", "s_fill", "s_hcopied"))
        s_a = [sem(f"s_a{j}") for j in range(K)]
        s_sa = [sem(f"s_sa{j}") for j in range(K)]
        s_t = [sem(f"s_t{j}") for j in range(K)]
        s_u = [sem(f"s_u{j}") for j in range(K)]
        s_cell = [sem(f"s_cell{j}") for j in range(K)]
        s_kept = [sem(f"s_kept{j}") for j in range(K)]
        s_th = [sem(f"s_th{j}") for j in range(K)]
        s_h = [sem(f"s_h{j}") for j in range(K)]
        s_ysq, s_dmp, s_sqrt, s_dm, s_wm, s_xn, s_y, s_yc, s_yd = (
            sem(n) for n in ("s_ysq", "s_dmp", "s_sqrt", "s_dm", "s_wm", "s_xn", "s_y", "s_yc", "s_yd"))

        block = ctx.enter_context(nc.Block())

        def chunk(q, j):
            return slice(q * D + j * P, q * D + (j + 1) * P)

        def hcols(ls, j):
            st, t = divmod(ls % BODY, T)
            return hst[:, st, j, (Q + B) * t:(Q + B) * t + B]

        @block.sync
        def _(sp):
            for n in range(B * XL):
                bb, lo = n // XL, n % XL * (TT // XL)
                sp.dma_start(xrow[:, bb, lo:lo + TT // XL, :],
                             x[bb, lo * P:(lo + TT // XL) * P, :].rearrange("(n p) d -> p n d", p=P)).then_inc(s_x[n], 16)
                if n == 0:
                    sp.dma_start(wx_sb[:, :, :], Wx.rearrange("(k p) g -> p k g", p=P)).then_inc(s_wx, 16)
                    sp.dma_start(wh_sb[:, :, :], Wh.rearrange("(k p) g -> p k g", p=P)).then_inc(s_wh, 16)
            for n in range(NX):
                bb, tt = n // TT, n % TT
                sp.wait_ge(s_yc, n + 1)
                sp.dma_start(out[bb, tt * P:(tt + 1) * P, :], ores[:, bb, tt, :]).then_inc(s_out, 16)
            sp.wait_ge(s_out, 16 * NX)

        @block.gpsimd
        def _(pool):
            pool.memset(ident[:, :], 0.0).then_inc(s_ms, 1)
            pool.wait_ge(s_ms, 1)
            pool.affine_select(out=ident[:, :], in_=ident[:, :], compare_op=ALU.not_equal, fill=1.0,
                               base=0, pattern=[[-1, P]], channel_multiplier=1).then_inc(s_id, 1)
            pool.memset(xT[:, :, SEQ:SEQ + T, :], 0.0).then_inc(s_xb, 1)
            for n in range(HC):
                pool.memset(ready[:, n:n + 1], 0.0).then_inc(s_hcopied, 1)
            pool.wait_ge(s_xTc, NXT)
            pool.tensor_copy(xblk[:, 0, :, :, :], xT[:, :, 0:T, :]).then_inc(s_xb, 1)
            with pool.Fori(0, NBLK // SETS) as it:
                i = it * SETS
                for st in range(SETS):
                    pool.wait_ge(s_fill, i + (st + 1))
                    pool.tensor_copy(xblk[:, 1 - st, :, :, :], xT[:, :, bass.ds((i + (st + 1)) * T, T), :]).then_inc(s_xb, 1)
                    for j in range(K):
                        pool.wait_ge(s_h[j], (i + (st + 1)) * T + 1)
                    for j in range(K):
                        diag = [hst[:, n, j, :].rearrange("p (t c) -> p t c", c=Q + B)[:, :, 0:B] for n in range(SETS)]
                        pool.tensor_copy(hist[:, bass.ds((i + st) * T, T - 1), j, :], diag[st][:, 1:T, :]).then_inc(s_hcopied, 1)
                        pool.tensor_copy(hist[:, bass.ds((i + st) * T + (T - 1), 1), j, :], diag[1 - st][:, 0:1, :]).then_inc(s_hcopied, 1)

        @block.scalar
        def _(act):
            for bb in range(B):
                act.dma_start(condT[:, :, bb], cond[bb, :].rearrange("(k p) -> p k", p=P),
                              allow_slow_non_contiguous=True).then_inc(s_c, 16)
            act.wait_ge(s_setup, 1)
            act.dma_start(bias_sb[0:1, :], b.rearrange("(a n) -> a n", a=1)).then_inc(s_b, 16)
            act.dma_start(w_sb[:, :, :], w.rearrange("(k p) o -> p k o", p=P)).then_inc(s_w, 16)
            act.wait_ge(s_dmp, 1)
            act.activation(dm[:, :, :], pX[0][:, :].rearrange("p (b d) -> p b d", b=B), ACT.Sqrt).then_inc(s_sqrt, 1)
            with act.Fori(0, SEQ, BODY) as i:
                for ls in range(BODY):
                    st, t = divmod(ls, T)
                    for j in range(K):
                        act.wait_ge(s_a[j], i + (ls + 1))
                        for lo in range(0, P, TM):
                            act.activation(gates[:, j, lo:lo + TM], pA[st][j][:, lo:lo + TM], ACT.Sigmoid).then_inc(s_sa[j], 1)
                    for j in range(K):
                        act.wait_ge(s_cell[j], i + (ls + 1))
                        act.activation(tanhc[:, j, :], pT[j][:, NT + 1:NT + NF:2], ACT.Tanh, scale=2.0).then_inc(s_th[j], 1)
            for n in range(NX):
                act.wait_ge(s_y, n + 1)
                act.activation(ores[:, n // TT, n % TT, :], pX[n % 2][:, 0:D], ACT.Copy).then_inc(s_yc, 1)

        @block.tensor
        def _(pe):
            pe.wait_ge(s_id, 1)
            for n in range(NX):
                if n % (TT // XL) == 0:
                    pe.wait_ge(s_x[n // (TT // XL)], 16)
                bb, tt = n // TT, n % TT
                for k in range(K):
                    m = n * K + k
                    if m >= 2:
                        pe.wait_ge(s_xTc, m - 1)
                    pe.transpose(pX[m % 2][:, 0:P], xrow[:, bb, tt, k * P:(k + 1) * P], ident[:, :]).then_inc(s_xT, 1)
            pe.wait_ge(s_ysq, 1)
            pe.wait_ge(s_xTc, NXT)
            for bb in range(B):
                for k in range(K):
                    last = pe.matmul(pX[0][:, bb * D:(bb + 1) * D], ysq[:, k, bb:bb + 1].broadcast_to([P, P]), wsq[:, k, :],
                                     start=(k == 0), stop=(k == K - 1))
            last.then_inc(s_dmp, 1)

            def fill(st, j, part):
                for q in range(G):
                    d = pA[st][j][q * Q:(q + 1) * Q, 0:P]
                    if part == 0:
                        last = pe.matmul(d, ones[:, :], bias_sb[:, chunk(q, j)], start=True, stop=False, skip_group_check=True)
                    else:
                        last = pe.matmul(d, xblk[:, st, part - 1, :, :], wx_sb[:, part - 1, chunk(q, j)], start=False,
                                         stop=False, skip_group_check=True)
                return last

            FILLS = [(j, part) for j in range(K) for part in range(1 + K)]

            def rec(st, t, j, k, lo=0, hi=P):
                M = B * (t + 1)
                for q in range(G):
                    last = pe.matmul(pA[st][j][q * Q:q * Q + M, lo:hi], hst[:, st, k, Q * t:Q * t + M],
                                     wh_sb[:, k, q * D + j * P + lo:q * D + j * P + hi],
                                     start=False, stop=True, skip_group_check=True)
                return last

            pe.wait_ge(s_scale, 3)
            pe.wait_ge(s_xb, 2)
            for j, part in FILLS:
                last = fill(0, j, part)
            last.then_inc(s_fill, 1)
            with pe.Fori(0, SEQ, BODY) as i:
                for ls in range(BODY):
                    st, t = divmod(ls, T)
                    pe.wait_ge(s_h[0], i + (ls + 1))
                    rec(st, t, 0, 0)
                    rec(st, t, 1, 0, 0, XS)
                    pe.wait_ge(s_h[1], i + (ls + 1))
                    rec(st, t, 0, 1).then_inc(s_a[0], 1)
                    rec(st, t, 1, 0, XS, P)
                    rec(st, t, 1, 1).then_inc(s_a[1], 1)
                    for j in range(K):
                        pe.wait_ge(s_kept[j], i + (ls + 1))
                        for n in range(P // TM):
                            lo = n * TM
                            pe.wait_ge(s_sa[j], (i + ls) * (P // TM) + (n + 1))
                            last = pe.matmul(pT[j][lo:lo + TM, 0:NT], gates[:, j, lo:lo + TM], sel[:, t, :], start=True, stop=True)
                        last.then_inc(s_t[j], 1)
                    n = t - (T - len(FILLS))
                    if n >= 0:
                        if n == 0:
                            pe.wait_ge(s_xb, i // T + (st + 3))
                        last = fill(1 - st, *FILLS[n])
                        if n == len(FILLS) - 1:
                            last.then_inc(s_fill, 1)
                    for _ in range(WARM - (n >= 0)):
                        pe.matmul(pX[0][0:Q, 0:P], ones[:, :], wh_sb[:, 0, 0:P], start=True, stop=True)
            pe.wait_ge(s_wm, B * K)
            for n in range(NX):
                bb, tt = n // TT, n % TT
                pe.wait_ge(s_xn, 1)
                if n >= 2:
                    pe.wait_ge(s_yc, n - 1)
                for k in range(K):
                    xs = xT[:, k, tt * P:(tt + 1) * P, bb]
                    pe.matmul(pX[n % 2][:, 0:D], xs, wmod[:, bb, k, :], start=(k == 0), stop=False, skip_group_check=True)
                for k in range(K):
                    xs = xT[:, k, tt * P:(tt + 1) * P, bb]
                    last = pe.matmul(pX[n % 2][:, k * P:(k + 1) * P], xs, ident[:, :], start=False, stop=(k == K - 1), skip_group_check=True)
                last.then_inc(s_y, 1)

        @block.vector
        def _(dve):
            dve.memset(bias_sb[:, :], 0.0).then_inc(s_setup, 1)
            dve.memset(ones[:, :], 1.0).then_inc(s_scale, 1)
            dve.memset(hst[:, :, :, :], 0.0).then_inc(s_setup, 1)
            dve.memset(sel[:, :, :], 0.0).then_inc(s_setup, 1)
            dve.memset(cell[:, :, :], 0.0).then_inc(s_setup, 1)
            dve.memset(ucst[:, :], 0.0).then_inc(s_setup, 1)
            dve.wait_ge(s_setup, 5)
            dve.memset(ucst[:, 0:NU:3], 1.0)
            dve.memset(ucst[:, 1:NU:3], -0.5).then_inc(s_setup, 1)
            dve.wait_ge(s_id, 1)
            for n, q, bb in SEL:
                dve.tensor_copy(sel[:, :, n], ident[:, q * Q + bb:(q + 1) * Q:B])
            for n in range(NX):
                bb, tt = n // TT, n % TT
                for k in range(K):
                    m = n * K + k
                    dve.wait_ge(s_xT, m + 1)
                    dve.tensor_copy(xT[:, k, tt * P:(tt + 1) * P, bb], pX[m % 2][:, 0:P]).then_inc(s_xTc, 1)
            dve.wait_ge(s_c, 16 * B)
            dve.tensor_scalar(yscale[:, :, :], condT[:, :, :], 1.0 / D ** 0.5, None, ALU.mult).then_inc(s_yd, 1)
            dve.wait_ge(s_yd, 1)
            dve.tensor_tensor(ysq[:, :, :], yscale[:, :, :], yscale[:, :, :], ALU.mult).then_inc(s_yd, 1)
            dve.wait_ge(s_yd, 2)
            dve.wait_ge(s_w, 16)
            dve.tensor_tensor(wsq[:, :, :], w_sb[:, :, :], w_sb[:, :, :], ALU.mult).then_inc(s_ysq, 1)
            dve.wait_ge(s_wx, 16)
            dve.wait_ge(s_wh, 16)
            dve.wait_ge(s_b, 16)
            gsl = slice(G_ * D, (G_ + 1) * D)
            dve.tensor_scalar(bias_sb[:, gsl], bias_sb[:, gsl], 2.0, None, ALU.mult)
            dve.tensor_scalar(wx_sb[:, :, gsl], wx_sb[:, :, gsl], 2.0, None, ALU.mult).then_inc(s_scale, 1)
            dve.tensor_scalar(wh_sb[:, :, gsl], wh_sb[:, :, gsl], 2.0, None, ALU.mult).then_inc(s_scale, 1)
            dve.wait_ge(s_sqrt, 1)
            dve.reciprocal(dm[:, :, :], dm[:, :, :]).then_inc(s_dm, 1)
            dve.wait_ge(s_dm, 1)
            for bb in range(B):
                for k in range(K):
                    dve.scalar_tensor_tensor(out=wmod[:, bb, k, :], in0=w_sb[:, k, :], scalar=yscale[:, k, bb:bb + 1],
                                             in1=dm[:, bb, :], op0=ALU.mult, op1=ALU.mult).then_inc(s_wm, 1)
            dve.wait_ge(s_wm, B * K)
            for j in range(K):
                dve.memset(tanhc[:, j, :], 0.0).then_inc(s_kept[j], 1)
                dve.tensor_copy(hcols(0, j), condT[:, j, :]).then_inc(s_h[j], 1)
            with dve.Fori(0, SEQ, BODY) as i:
                for ls in range(BODY):
                    st, t = divmod(ls, T)
                    par = ls % 2
                    if ls == T - 1:
                        dve.wait_ge(s_hcopied, i // T * HC + HC)
                    if ls == BODY - 1:
                        dve.wait_ge(s_hcopied, i // T * HC + 2 * HC)
                    for step, j in (("u", 0), ("cell", 0), ("u", 1), ("h", 0), ("cell", 1), ("keep", 0), ("h", 1), ("keep", 1)):
                        if step == "u":
                            dve.wait_ge(s_t[j], i + (ls + 1))
                            dve.tensor_tensor_scan(cell[:, j, C0:C0 + 11:2], pT[j][:, 0:NU], ucst[:, :], 0.0,
                                                   ALU.mult, ALU.add).then_inc(s_u[j], 1)
                        elif step == "cell":
                            dve.wait_ge(s_u[j], i + (ls + 1))
                            dve.tensor_tensor_scan(pT[j][:, NT:NT + NF], pT[j][:, NU:NU + NF],
                                                   cell[:, j, C0 + 1:C0 + 11:3], 0.0, ALU.mult, ALU.add).then_inc(s_cell[j], 1)
                        elif step == "keep":
                            dve.wait_ge(s_cell[j], i + (ls + 1))
                            dve.tensor_copy(cell[:, j, C0 + 1:C0 + 8:6], pT[j][:, NT + 1:NT + NF:2]).then_inc(s_kept[j], 1)
                        else:
                            dve.wait_ge(s_th[j], i + (ls + 1))
                            dve.tensor_tensor(hcols(ls + 1, j), tanhc[:, j, :], pT[j][:, NU + NF:NT], ALU.mult).then_inc(s_h[j], 1)
            dve.wait_ge(s_hcopied, (NBLK + 1) * HC)
            dve.tensor_tensor(xT[:, :, 0:SEQ, :], xT[:, :, 0:SEQ, :], hist[:, :, :, :].rearrange("p t k b -> p k t b"),
                              ALU.add).then_inc(s_xn, 1)


_INS = ['x', 'cond_1024', 'L0_cond_Wx', 'L0_cond_Wh', 'L0_cond_b', 'L1_cond_weight']
_OUTS = [((2, 1024, 256), 'float32')]


def kernel(**inputs):
    import numpy as _np
    import concourse.bacc as _bacc
    from concourse import mybir as _mybir
    from concourse.bass_utils import run_bass_kernel_spmd as _run

    nc = _bacc.Bacc("TRN2", target_bir_lowering=False, num_devices=1)
    arrays, args = {}, []
    for name in _INS:
        a = _np.ascontiguousarray(inputs[name])
        arrays[f"in_{name}_dram"] = a
        args.append(nc.dram_tensor(f"in_{name}_dram", a.shape, _mybir.dt.from_np(a.dtype), kind="ExternalInput").ap())
    for i, (shape, dtype) in enumerate(_OUTS):
        dt = _mybir.dt.from_np(_np.dtype(dtype))
        args.append(nc.dram_tensor(f"out_{i}_dram", shape, dt, kind="ExternalOutput").ap())
    build(nc, *args)
    r = _run(nc, [arrays], core_ids=[0])
    got = tuple(r.results[0][f"out_{i}_dram"] for i in range(len(_OUTS)))
    return got[0]
```

```python
import concourse.bass as bass
from concourse import mybir
from contextlib import ExitStack

P = 128
EPS = 1e-8
F32 = mybir.dt.float32
ACT = mybir.ActivationFunctionType
ALU = mybir.AluOpType


def build(nc, x, cond, Wx, Wh, b, w, out):
    B, SEQ, D = x.shape
    K = D // P
    G = 4
    Q = P // G
    T = 8
    ROWS = T * B
    SETS = 2
    NB = 8
    BODY = NB * T
    R = BODY
    NBODY = SEQ // BODY
    I_, F_, O_, G_ = range(G)
    NU, NF = 3 * B, 2 * B
    NT = NU + NF + B
    SEL = ([(3 * bb + 1, G_, bb) for bb in range(B)] + [(3 * bb + 2, I_, bb) for bb in range(B)]
           + [(NU + 2 * bb + 1, F_, bb) for bb in range(B)] + [(NU + NF + bb, O_, bb) for bb in range(B)])
    C0 = 3
    CELL_COLS = 16
    SCAN1_OUT = slice(C0, C0 + 2 * NU - 1, 2)
    SCAN2_IN = slice(C0 + 1, C0 + 1 + 3 * NF - 2, 3)
    CELL_IN = slice(C0 + 1, C0 + 1 + 6 * B - 5, 6)

    XSTEP = 1
    YSTEPS = list(range(2, 8))
    YDONE = YSTEPS[-1] + 1
    PRODUCTS = 2
    HEAD = 64
    PIECE = 64
    PIECES = P // PIECE
    HC = 2 * K

    ctx = ExitStack()
    with ctx:
        def sb(name, shape):
            return ctx.enter_context(nc.sbuf_tensor(name, shape, F32))

        def sem(name):
            return ctx.enter_context(nc.semaphore(name))

        wx_sb = sb("wx_sb", [P, K, G * D])
        wh_sb = sb("wh_sb", [P, K, G * D])
        bias_sb = sb("bias_sb", [P, G * D])
        ones = sb("ones", [P, Q])
        ident = sb("ident", [P, P])
        sel = sb("sel", [P, T, NT])
        xin = sb("xin", [P, D])
        xT = sb("xT", [P, K, SEQ + R, B])
        xblk = sb("xblk", [P, SETS, K, T, B])
        hst = sb("hst", [P, SETS, K, T * (Q + B)])
        xh = sb("xh", [P, K, B, R])
        gates = sb("gates", [P, K, P])
        scan1_add = sb("scan1_add", [P, NU])
        cell = sb("cell", [P, K, CELL_COLS])
        warmed = sb("warmed", [P, 1])
        tanhc = sb("tanhc", [P, K, B])
        condT = sb("condT", [P, K, B])
        ysq = sb("ysq", [P, K, B])
        yscale = sb("yscale", [P, K, B])
        w_sb = sb("w_sb", [P, K, D])
        wsq = sb("wsq", [P, K, D])
        demod = sb("demod", [P, B, D])
        wmod = sb("wmod", [P, B, K, D])
        ores = sb("ores", [P, NBODY + 1, D])

        pA = [[ctx.enter_context(nc.psum_tensor(f"pA{s}{j}", [P, 512], F32)) for j in range(K)] for s in range(SETS)]
        pT = [ctx.enter_context(nc.psum_tensor(f"pT{j}", [P, 512], F32)) for j in range(K)]
        pX = [ctx.enter_context(nc.psum_tensor(f"pX{s}", [P, 512], F32)) for s in range(2)]

        x_loaded, cond_loaded, w_loaded, wx_loaded, wh_loaded, bias_loaded, out_written = (sem(n) for n in (
            "x_loaded", "cond_loaded", "w_loaded", "wx_loaded", "wh_loaded", "bias_loaded", "out_written"))
        buffers_zeroed, ident_zeroed, ident_ready, operands_ready = (sem(n) for n in (
            "buffers_zeroed", "ident_zeroed", "ident_ready", "operands_ready"))
        ys_ready, squares_ready, demod_summed, demod_added, demod_rooted, demod_ready, wmod_ready = (sem(n) for n in (
            "ys_ready", "squares_ready", "demod_summed", "demod_added", "demod_rooted", "demod_ready", "wmod_ready"))
        x_transposed, xT_ready, xblk_ready, block_filled = (sem(n) for n in (
            "x_transposed", "xT_ready", "xblk_ready", "block_filled"))
        xh_ready, result_summed, result_ready = (sem(n) for n in ("xh_ready", "result_summed", "result_ready"))
        sums_ready = [sem(f"sums_ready{j}") for j in range(K)]
        sigmoids_ready = [sem(f"sigmoids_ready{j}") for j in range(K)]
        gates_transposed = [sem(f"gates_transposed{j}") for j in range(K)]
        u_ready = [sem(f"u_ready{j}") for j in range(K)]
        cell_ready = [sem(f"cell_ready{j}") for j in range(K)]
        cells_kept = sem("cells_kept")
        tanh_ready = [sem(f"tanh_ready{j}") for j in range(K)]
        h_ready = [sem(f"h_ready{j}") for j in range(K)]

        block = ctx.enter_context(nc.Block())

        def chunk(q, j):
            return slice(q * D + j * P, q * D + (j + 1) * P)

        def hcols(ls, j):
            blk, t = divmod(ls, T)
            return hst[:, blk % SETS, j, (Q + B) * t:(Q + B) * t + B]

        @block.sync
        def _(sp):
            def load(body):
                for bb in range(B):
                    sp.dma_start(xin[bb * R:(bb + 1) * R, :], x[bb, bass.ds(body * R, R), :]).then_inc(x_loaded, 16)

            def store(body):
                for bb in range(B):
                    sp.dma_start(out[bb, bass.ds(body * R, R), :],
                                 ores[bb * R:(bb + 1) * R, bass.ds(body + 1, 1), :].rearrange("p o d -> p (o d)")
                                 ).then_inc(out_written, 16)

            load(0)
            sp.dma_start(w_sb[:, :, :], w.rearrange("(k p) o -> p k o", p=P)).then_inc(w_loaded, 16)
            sp.dma_start(wx_sb[:, :, :], Wx.rearrange("(k p) g -> p k g", p=P)).then_inc(wx_loaded, 16)
            for body in (1, 2):
                sp.wait_ge(x_transposed, K * body)
                load(body)
            with sp.Fori(1, NBODY - 2) as it:
                sp.wait_ge(x_transposed, it * K + 2 * K)
                load(it + 2)
                sp.wait_ge(result_ready, it + 1)
                store(it - 1)
            sp.wait_ge(x_transposed, NBODY * K)
            load(NBODY - 1)
            for body in range(NBODY - 3, NBODY):
                sp.wait_ge(result_ready, body + 2)
                store(body)
            sp.wait_ge(out_written, 16 * B * NBODY)

        @block.gpsimd
        def _(pool):
            pool.memset(ident[:, :], 0.0).then_inc(ident_zeroed, 1)
            pool.wait_ge(ident_zeroed, 1)
            pool.affine_select(out=ident[:, :], in_=ident[:, :], compare_op=ALU.not_equal, fill=1.0,
                               base=0, pattern=[[-1, P]], channel_multiplier=1).then_inc(ident_ready, 1)
            for n in range(HC):
                pool.memset(xh[:, n // 2, :, n % 2 * (R // 2):(n % 2 + 1) * (R // 2)], 0.0).then_inc(xh_ready, 1)
            pool.wait_ge(xT_ready, K)
            pool.tensor_copy(xblk[:, 0, :, :, :], xT[:, :, 0:T, :]).then_inc(xblk_ready, 1)
            with pool.Fori(0, NBODY) as it:
                for n in range(NB):
                    st = n % SETS
                    blk = it * NB + n
                    pool.wait_ge(block_filled, blk + 1)
                    pool.wait_ge(xh_ready, blk * HC + HC)
                    if n == NB - 1:
                        pool.wait_ge(xT_ready, it * K + 2 * K)
                    pool.tensor_copy(xblk[:, 1 - st, :, :, :],
                                     xT[:, :, bass.ds((it * NB + (n + 1)) * T, T), :]).then_inc(xblk_ready, 1)
                    for j in range(K):
                        pool.wait_ge(h_ready[j], (it * NB + (n + 1)) * T + 1)
                    if n == 0:
                        pool.wait_ge(result_summed, it + 1)
                    for j in range(K):
                        diag = [hst[:, m, j, :].rearrange("p (t c) -> p t c", c=Q + B)[:, :, 0:B] for m in range(SETS)]
                        xhj = xh[:, j, :, n * T:(n + 1) * T].rearrange("p b t -> p t b")
                        pool.tensor_tensor(xhj[:, 0:T - 1, :], xblk[:, st, j, 0:T - 1, :],
                                           diag[st][:, 1:T, :], ALU.add).then_inc(xh_ready, 1)
                        pool.tensor_tensor(xhj[:, T - 1:T, :], xblk[:, st, j, T - 1:T, :],
                                           diag[1 - st][:, 0:1, :], ALU.add).then_inc(xh_ready, 1)

        @block.scalar
        def _(act):
            for bb in range(B):
                act.dma_start(condT[:, :, bb], cond[bb, :].rearrange("(k p) -> p k", p=P),
                              allow_slow_non_contiguous=True).then_inc(cond_loaded, 16)
            act.wait_ge(buffers_zeroed, 1)
            act.dma_start(bias_sb[0:1, :], b.rearrange("(a n) -> a n", a=1)).then_inc(bias_loaded, 16)
            act.dma_start(wh_sb[:, :, :], Wh.rearrange("(k p) g -> p k g", p=P)).then_inc(wh_loaded, 16)
            act.wait_ge(demod_added, 1)
            act.activation(demod[:, :, :], demod[:, :, :], ACT.Sqrt).then_inc(demod_rooted, 1)
            act.activation(warmed[:, :], ones[:, 0:1], ACT.Sigmoid)

            def result(slot):
                act.wait_ge(result_summed, slot + 1)
                act.activation(ores[:, bass.ds(slot, 1), :].rearrange("p o d -> p (o d)"), pX[0][:, 0:D],
                               ACT.Copy).then_inc(result_ready, 1)

            with act.Fori(0, NBODY) as it:
                i = it * BODY
                for ls in range(BODY):
                    st, t = divmod(ls, T)
                    st %= SETS
                    for j in range(K):
                        act.wait_ge(sums_ready[j], i + (ls + 1))
                        for lo in range(0, P, PIECE):
                            act.activation(gates[:, j, lo:lo + PIECE], pA[st][j][:, lo:lo + PIECE],
                                           ACT.Sigmoid).then_inc(sigmoids_ready[j], 1)
                    for j in range(K):
                        act.wait_ge(cell_ready[j], i + (ls + 1))
                        act.activation(tanhc[:, j, :], pT[j][:, NT + 1:NT + NF:2], ACT.Tanh,
                                       scale=2.0).then_inc(tanh_ready[j], 1)
                    if ls == YDONE:
                        result(it)
            result(NBODY)

        @block.tensor
        def _(pe):
            def transposes(k):
                pe.transpose(pX[1][:, k * P:(k + 1) * P], xin[:, k * P:(k + 1) * P], ident[:, :]).then_inc(x_transposed, 1)

            pe.wait_ge(ident_ready, 1)
            pe.wait_ge(x_loaded, 16 * B)
            for k in range(K):
                transposes(k)
            pe.wait_ge(squares_ready, 1)
            for bb in range(B):
                for k in range(K):
                    last = pe.matmul(pX[0][:, bb * D:(bb + 1) * D], ysq[:, k, bb:bb + 1].broadcast_to([P, P]), wsq[:, k, :],
                                     start=(k == 0), stop=(k == K - 1))
            last.then_inc(demod_summed, 1)

            def filler(bank):
                pe.matmul(pX[bank][0:Q, 3 * P:4 * P], ones[:, :], wh_sb[:, 0, 0:P], start=True, stop=True)

            def fill(st, j, part):
                for q in range(G):
                    if part == 0:
                        last = pe.matmul(pA[st][j][q * Q:(q + 1) * Q, 0:P], ones[:, :], bias_sb[:, chunk(q, j)],
                                         start=True, stop=False, skip_group_check=True)
                    else:
                        last = pe.matmul(pA[st][j][q * Q:q * Q + ROWS, 0:P], xblk[:, st, part - 1, :, :],
                                         wx_sb[:, part - 1, chunk(q, j)], start=False, stop=False, skip_group_check=True)
                return last

            FILLS = [(j, part) for j in range(K) for part in range(1 + K)]

            def rec(st, t, j, k, lo=0, hi=P):
                M = B * (t + 1)
                for q in range(G):
                    last = pe.matmul(pA[st][j][q * Q:q * Q + M, lo:hi], hst[:, st, k, Q * t:Q * t + M],
                                     wh_sb[:, k, q * D + j * P + lo:q * D + j * P + hi],
                                     start=False, stop=True, skip_group_check=True)
                return last

            pe.wait_ge(operands_ready, 4)
            pe.wait_ge(xblk_ready, 1)
            for j, part in FILLS:
                last = fill(0, j, part)
            last.then_inc(block_filled, 1)
            for _ in range(24):
                filler(1)

            LAYER = ([(k, wmod, lo) for k in range(K) for lo in range(0, D, P)] + [(k, ident, k * P) for k in range(K)])

            def layer(n):
                k, what, lo = LAYER[n]
                for bb in range(B):
                    rhs = ident[:, :] if what is ident else wmod[:, bb, k, lo:lo + P]
                    last = pe.matmul(pX[0][bb * R:(bb + 1) * R, lo:lo + P], xh[:, k, bb, :], rhs, start=(n == 0),
                                     stop=(n == len(LAYER) - 1), skip_group_check=True)
                if n == len(LAYER) - 1:
                    last.then_inc(result_summed, 1)

            with pe.Fori(0, NBODY) as it:
                i = it * BODY
                for ls in range(BODY):
                    blk, t = divmod(ls, T)
                    st = blk % SETS
                    pe.wait_ge(h_ready[0], i + (ls + 1))
                    rec(st, t, 0, 0)
                    rec(st, t, 1, 0, 0, HEAD)
                    pe.wait_ge(h_ready[1], i + (ls + 1))
                    rec(st, t, 0, 1).then_inc(sums_ready[0], 1)
                    rec(st, t, 1, 0, HEAD, P)
                    pe.wait_ge(cells_kept, i + (ls + 1))
                    rec(st, t, 1, 1).then_inc(sums_ready[1], 1)
                    for j in range(K):
                        for n in range(PIECES):
                            lo = n * PIECE
                            pe.wait_ge(sigmoids_ready[j], (i + ls) * PIECES + (n + 1))
                            last = pe.matmul(pT[j][lo:lo + PIECE, 0:NT], gates[:, j, lo:lo + PIECE], sel[:, t, :],
                                             start=True, stop=True)
                        last.then_inc(gates_transposed[j], 1)
                    work = 0
                    n = t - (T - len(FILLS))
                    if n >= 0:
                        work = 1
                        if n == 0:
                            pe.wait_ge(xblk_ready, it * NB + (blk + 2))
                        last = fill(1 - st, *FILLS[n])
                        if n == len(FILLS) - 1:
                            last.then_inc(block_filled, 1)
                    if ls == XSTEP:
                        pe.wait_ge(x_loaded, it * (16 * B) + 2 * 16 * B)
                        for k in range(K):
                            transposes(k)
                    if ls in YSTEPS:
                        work += 1
                        if ls == YSTEPS[0]:
                            pe.wait_ge(xh_ready, it * (NB * HC) + HC)
                        layer(YSTEPS.index(ls))
                    for _ in range(PRODUCTS - work):
                        filler(0 if ls < YSTEPS[0] else 1)
            pe.wait_ge(xh_ready, (NBODY * NB + 1) * HC)
            for n in range(len(LAYER)):
                layer(n)

        @block.vector
        def _(dve):
            dve.memset(bias_sb[:, :], 0.0).then_inc(buffers_zeroed, 1)
            dve.memset(ones[:, :], 1.0).then_inc(operands_ready, 1)
            dve.memset(hst[:, :, :, :], 0.0).then_inc(buffers_zeroed, 1)
            dve.memset(sel[:, :, :], 0.0).then_inc(buffers_zeroed, 1)
            dve.memset(cell[:, :, :], 0.0).then_inc(buffers_zeroed, 1)
            dve.memset(scan1_add[:, :], 0.0).then_inc(buffers_zeroed, 1)
            dve.wait_ge(buffers_zeroed, 5)
            dve.memset(scan1_add[:, 0:NU:3], 1.0)
            dve.memset(scan1_add[:, 1:NU:3], -0.5)
            dve.wait_ge(ident_ready, 1)
            for n, q, bb in SEL:
                dve.tensor_copy(sel[:, :, n], ident[:, q * Q + bb:q * Q + ROWS:B])

            def untangle(k, row):
                dve.wait_ge(x_transposed, row // R * K + K)
                dve.tensor_copy(xT[:, k, bass.ds(row, R), :].rearrange("p t b -> p b t"),
                                pX[1][:, k * P:(k + 1) * P].rearrange("p (b t) -> p b t", b=B)).then_inc(xT_ready, 1)

            for k in range(K):
                untangle(k, 0)
            dve.wait_ge(cond_loaded, 16 * B)
            dve.tensor_scalar(yscale[:, :, :], condT[:, :, :], 1.0 / D ** 0.5, None, ALU.mult).then_inc(ys_ready, 1)
            dve.wait_ge(ys_ready, 1)
            dve.tensor_tensor(ysq[:, :, :], yscale[:, :, :], yscale[:, :, :], ALU.mult)
            dve.wait_ge(w_loaded, 16)
            dve.tensor_tensor(wsq[:, :, :], w_sb[:, :, :], w_sb[:, :, :], ALU.mult).then_inc(squares_ready, 1)
            g_cols = slice(G_ * D, (G_ + 1) * D)
            dve.wait_ge(bias_loaded, 16)
            dve.tensor_scalar(bias_sb[:, g_cols], bias_sb[:, g_cols], 2.0, None, ALU.mult).then_inc(operands_ready, 1)
            dve.wait_ge(wx_loaded, 16)
            dve.tensor_scalar(wx_sb[:, :, g_cols], wx_sb[:, :, g_cols], 2.0, None, ALU.mult).then_inc(operands_ready, 1)
            dve.wait_ge(wh_loaded, 16)
            dve.tensor_scalar(wh_sb[:, :, g_cols], wh_sb[:, :, g_cols], 2.0, None, ALU.mult).then_inc(operands_ready, 1)
            dve.wait_ge(demod_summed, 1)
            dve.tensor_scalar(demod[:, :, :], pX[0][:, :].rearrange("p (b d) -> p b d", b=B), EPS, None,
                              ALU.add).then_inc(demod_added, 1)
            dve.wait_ge(demod_rooted, 1)
            dve.reciprocal(demod[:, :, :], demod[:, :, :]).then_inc(demod_ready, 1)
            dve.wait_ge(demod_ready, 1)
            for bb in range(B):
                for k in range(K):
                    dve.scalar_tensor_tensor(out=wmod[:, bb, k, :], in0=w_sb[:, k, :], scalar=yscale[:, k, bb:bb + 1],
                                             in1=demod[:, bb, :], op0=ALU.mult, op1=ALU.mult).then_inc(wmod_ready, 1)
            dve.wait_ge(wmod_ready, B * K)
            dve.memset(tanhc[:, :, :], 0.0).then_inc(cells_kept, 1)
            for j in range(K):
                dve.tensor_copy(hcols(0, j), condT[:, j, :]).then_inc(h_ready[j], 1)
            with dve.Fori(0, NBODY) as it:
                i = it * BODY
                for ls in range(BODY):
                    blk, t = divmod(ls, T)
                    if t == T - 1:
                        dve.wait_ge(xh_ready, it * (NB * HC) + (blk + 1) * HC)
                    for step, j in (("u", 0), ("cell", 0), ("u", 1), ("h", 0), ("cell", 1), ("keep", 0), ("h", 1),
                                    ("keep", 1)):
                        if step == "u":
                            dve.wait_ge(gates_transposed[j], i + (ls + 1))
                            dve.tensor_tensor_scan(cell[:, j, SCAN1_OUT], pT[j][:, 0:NU], scan1_add[:, :], 0.0,
                                                   ALU.mult, ALU.add).then_inc(u_ready[j], 1)
                        elif step == "cell":
                            dve.wait_ge(u_ready[j], i + (ls + 1))
                            dve.tensor_tensor_scan(pT[j][:, NT:NT + NF], pT[j][:, NU:NU + NF],
                                                   cell[:, j, SCAN2_IN], 0.0, ALU.mult, ALU.add).then_inc(cell_ready[j], 1)
                        elif step == "keep":
                            dve.wait_ge(cell_ready[j], i + (ls + 1))
                            keep = dve.tensor_copy(cell[:, j, CELL_IN], pT[j][:, NT + 1:NT + NF:2])
                            if j == K - 1:
                                keep.then_inc(cells_kept, 1)
                        else:
                            dve.wait_ge(tanh_ready[j], i + (ls + 1))
                            dve.tensor_tensor(hcols(ls + 1, j), tanhc[:, j, :], pT[j][:, NU + NF:NT],
                                              ALU.mult).then_inc(h_ready[j], 1)
                    if ls == XSTEP + 1:
                        for k in range(K):
                            untangle(k, (it + 1) * R)


_INS = ['x', 'cond_1024', 'L0_cond_Wx', 'L0_cond_Wh', 'L0_cond_b', 'L1_cond_weight']
_OUTS = [((2, 1024, 256), 'float32')]


def kernel(**inputs):
    import numpy as _np
    import concourse.bacc as _bacc
    from concourse import mybir as _mybir
    from concourse.bass_utils import run_bass_kernel_spmd as _run

    nc = _bacc.Bacc("TRN2", target_bir_lowering=False, num_devices=1)
    arrays, args = {}, []
    for name in _INS:
        a = _np.ascontiguousarray(inputs[name])
        arrays[f"in_{name}_dram"] = a
        args.append(nc.dram_tensor(f"in_{name}_dram", a.shape, _mybir.dt.from_np(a.dtype), kind="ExternalInput").ap())
    for i, (shape, dtype) in enumerate(_OUTS):
        dt = _mybir.dt.from_np(_np.dtype(dtype))
        args.append(nc.dram_tensor(f"out_{i}_dram", shape, dt, kind="ExternalOutput").ap())
    build(nc, *args)
    r = _run(nc, [arrays], core_ids=[0])
    got = tuple(r.results[0][f"out_{i}_dram"] for i in range(len(_OUTS)))
    return got[0]
```
